# Optimizing a Trainium2 kernel written in Bass

```python
import numpy as np
import jax
import jax.numpy as jnp

def _softmax(x, axis=-1):
    return jax.nn.softmax(x, axis=axis)
def _gelu(x):
    return jax.nn.gelu(x, approximate=True)
def _silu(x):
    return jax.nn.silu(x)
def _sigmoid(x):
    return jax.nn.sigmoid(x)
def _layernorm(x, axis=-1, eps=1e-5):
    m = jnp.mean(x, axis=axis, keepdims=True)
    v = jnp.var(x, axis=axis, keepdims=True)
    return (x - m) / jnp.sqrt(v + eps)
def _scatter_add(tgt, idx, src, axis=0):
    return tgt.at[idx].add(src)
def _segment_sum(src, seg, n):
    return jax.ops.segment_sum(src, seg, n)

kernel_name = 'mk_rec_standalone_d1_rec_5a872a'

def setup_inputs(seed: int = 0):
    np.random.seed(seed)
    _w = jnp.asarray
    def _rec_inputs():
        import jax
        import jax.numpy as jnp
        _rk = jax.random.key(seed)
        r_inputs = -7.10856e-05 + 0.999911 * jax.random.normal(jax.random.fold_in(_rk, 1), (16384, 4096), jnp.float32)
        return r_inputs
    r_inputs = _rec_inputs()
    def _L0_rec_setup():
        import jax, jax.numpy as jnp
        import numpy as np
        B, D, L = (16384, 4096, 6)
        key = jax.random.key(seed)
        k_x, k_w = jax.random.split(key)
        inputs = jax.random.normal(k_x, (B, D), dtype=jnp.float32)
        bound = float(np.sqrt(6.0 / (D + 1)))
        w = jax.random.uniform(k_w, (L, D, 1), dtype=jnp.float32, minval=-bound, maxval=bound)
        b = jnp.zeros((L, D), dtype=jnp.float32)
        return {'inputs': inputs, 'w': w, 'b': b}
    _L0_rec_all = _L0_rec_setup()
    _L0_rec_in = {k: v for k, v in _L0_rec_all.items() if k in ('w', 'b', )}
    del _L0_rec_all

    return {
        "r_inputs": r_inputs,
        "L0_rec_w": _L0_rec_in["w"],
        "L0_rec_b": _L0_rec_in["b"],
    }

def reference(r_inputs, L0_rec_w, L0_rec_b):
    import jax
    import jax.numpy as jnp
    def _L0_rec_ref(inputs, w, b):
        import jax, jax.numpy as jnp
        import numpy as np
        B, D, L = (16384, 4096, 6)
        x0 = inputs

        def step(x, wb):
            wi, bi = wb
            xw = jnp.matmul(x, wi)
            x_new = x0 * xw + bi + x
            return (x_new, None)
        x, _ = jax.lax.scan(step, inputs, (w, b))
        return x

    y = _L0_rec_ref(r_inputs, L0_rec_w, L0_rec_b)
    return y


_drawn_inputs = setup_inputs


def setup_inputs(seed=0):
    import zlib

    import numpy as np

    out = dict(_drawn_inputs(seed))
    spreads = {'L0_rec_b': (0.0, 0.1)}
    factors = {}
    for name, (base, spread) in spreads.items():
        noise = np.random.default_rng([zlib.crc32(name.encode()), seed]).standard_normal(out[name].shape)
        drawn = base * np.exp(spread * noise) if base else spread * noise
        out[name] = jnp.asarray(drawn.astype(out[name].dtype))
    for name, factor in factors.items():
        out[name] = (out[name] * factor).astype(out[name].dtype)
    return out
```

```python
from contextlib import ExitStack

import concourse.bass as bass
from concourse import mybir

F32 = mybir.dt.float32
ALU = mybir.AluOpType
ACT = mybir.ActivationFunctionType

P = 128
Q = 32
G = P // Q
TB = 4
NCHUNK = 4
LP = 8
BANK = 512
HALF_BANKS = 4


def cross_network(nc, x, w, b, out):
    rows, D = x.shape
    L = w.shape[0]
    n_tiles = rows // P
    n_batches = n_tiles // TB
    n_slots = 2 * TB
    n_rounds = n_batches // 2
    CH = D // NCHUNK
    KB = CH // Q
    HALF = HALF_BANKS * BANK
    n_halves = D // HALF
    assert L <= LP and G * LP == Q and n_batches % 2 == 0 and D % HALF == 0 and CH % (Q * G) == 0

    w_rows = w.rearrange("l d a -> l (d a)")

    with ExitStack() as ctx:
        def sb(name, shape):
            return ctx.enter_context(nc.sbuf_tensor(name, shape, F32))

        def ps(name, shape):
            return ctx.enter_context(nc.psum_tensor(name, shape, F32))

        def sem(name):
            return ctx.enter_context(nc.semaphore(name))

        tiles = sb("tiles", [P, n_slots, D])
        blocks = sb("blocks", [P, 2, TB, CH])
        weights = sb("weights", [P, D // Q, Q])
        c_last = sb("c_last", [P, D])
        ones = sb("ones", [P, P])
        earlier = sb("earlier", [L, LP])
        ident = sb("ident", [L, LP])
        group_mask = sb("group_mask", [P, G])
        lanes = sb("lanes", [P, P // LP])
        layer_sel = sb("layer_sel", [P, LP])
        cw_part = sb("cw_part", [L, n_halves])
        cw_sum = sb("cw_sum", [L, 1])
        cw_diag = sb("cw_diag", [L, LP])
        cw = sb("cw", [P, LP])
        spread = sb("spread", [P, TB, G, Q])
        growth = sb("growth", [P, TB, LP])
        scale = sb("scale", [P, 2, TB, LP])

        w_stage = tiles[:, n_slots - 1, :]
        b_stage = tiles[0:L, n_slots - 2, :]
        cw_prod = tiles[0:L, n_slots - 3, :]

        dots = ps("dots", [P, TB, Q])
        turned = ps("turned", [P, TB, LP])
        scratch = ps("scratch", [P, HALF])

        x_landed = [sem(f"x_landed{s}") for s in range(n_slots)]
        y_stored = [sem(f"y_stored{s}") for s in range(n_slots)]
        w_landed = [sem(f"w_landed{g}") for g in range(G)]
        b_landed = sem("b_landed")
        stage_zeroed = sem("stage_zeroed")
        ones_ready = sem("ones_ready")
        zeros_ready = sem("zeros_ready")
        masks_built = sem("masks_built")
        weights_ready = sem("weights_ready")
        group_mask_ready = sem("group_mask_ready")
        scratch_filled = sem("scratch_filled")
        products_summed = sem("products_summed")
        cw_summed = sem("cw_summed")
        cw_diag_ready = sem("cw_diag_ready")
        scratch_copied = sem("scratch_copied")
        blocks_ready = sem("blocks_ready")
        blocks_used = sem("blocks_used")
        dots_spread = sem("dots_spread")
        turned_ready = sem("turned_ready")
        growth_ready = sem("growth_ready")
        scale_ready = sem("scale_ready")
        tiles_done = sem("tiles_done")

        block = ctx.enter_context(nc.Block())

        @block.sync
        def _(sp):
            sp.wait_ge(stage_zeroed, 2)
            for g in range(G):
                at = g * Q + g * LP
                sp.dma_start(w_stage[at:at + L, :], w_rows).then_inc(w_landed[g], 16)
            sp.dma_start(b_stage, b).then_inc(b_landed, 16)
            for s in range(n_slots):
                if s == n_slots - 3:
                    sp.wait_ge(products_summed, n_halves)
                    sp.wait_ge(scratch_filled, 2 * n_halves)
                    sp.wait_ge(weights_ready, 1)
                sp.dma_start(tiles[:, s, :], x[s * P:(s + 1) * P, :]).then_inc(x_landed[s], 16)
            with sp.Fori(1, n_rounds) as r:
                for s in range(n_slots):
                    sp.wait_ge(y_stored[s], r * 16)
                    sp.dma_start(tiles[:, s, :], x[bass.ds((r * n_slots + s) * P, P), :]).then_inc(x_landed[s], 16)

        @block.gpsimd
        def _(pool):
            nc.gpsimd.memset(w_stage[:, 0:D // 2], 0.0).then_inc(stage_zeroed, 1)
            nc.gpsimd.memset(layer_sel[:], 0.0).then_inc(zeros_ready, 1)
            nc.gpsimd.memset(ident[:], 0.0).then_inc(zeros_ready, 1)
            pool.wait_ge(ones_ready, 1)
            nc.gpsimd.affine_select(out=earlier[:], in_=ones[0:L, 0:LP], compare_op=ALU.is_ge, fill=0.0,
                                    base=-1, pattern=[[1, LP]], channel_multiplier=-1).then_inc(masks_built, 1)
            pool.wait_ge(zeros_ready, 2)
            nc.gpsimd.affine_select(out=ident[:], in_=ident[:], compare_op=ALU.not_equal, fill=1.0,
                                    base=0, pattern=[[-1, LP]], channel_multiplier=1).then_inc(masks_built, 1)
            for q in range(P // LP):
                nc.gpsimd.affine_select(out=layer_sel[:], in_=layer_sel[:], compare_op=ALU.not_equal, fill=1.0,
                                        base=-q * LP, pattern=[[-1, LP]],
                                        channel_multiplier=1).then_inc(masks_built, 1)
                pool.wait_ge(masks_built, 3 + q)
            nc.gpsimd.affine_select(out=lanes[:], in_=ones[:, 0:P // LP], compare_op=ALU.is_ge, fill=0.0,
                                    base=0, pattern=[[-LP, P // LP]],
                                    channel_multiplier=1).then_inc(masks_built, 1)
            pool.wait_ge(masks_built, 3 + P // LP)
            nc.gpsimd.affine_select(out=lanes[:], in_=lanes[:], compare_op=ALU.is_ge, fill=0.0,
                                    base=LP - 1, pattern=[[LP, P // LP]],
                                    channel_multiplier=-1).then_inc(masks_built, 1)

        @block.scalar
        def _(act):
            for h in range(n_halves):
                act.wait_ge(scratch_filled, n_halves + h + 1)
                nc.scalar.copy(c_last[:, h * HALF:(h + 1) * HALF], scratch[:]).then_inc(scratch_copied, 1)
            act.wait_ge(scratch_filled, 2 * n_halves + 1)
            nc.scalar.copy(cw[:], scratch[:, 0:LP]).then_inc(scratch_copied, 1)

            def make_growth(batch, first=False):
                act.wait_ge(blocks_used, (batch + 1) * NCHUNK)
                if first:
                    act.wait_ge(group_mask_ready, 1)
                for g in range(G):
                    nc.scalar.activation(spread[:, :, g, :], dots[:], ACT.Copy,
                                         scale=group_mask[:, g:g + 1]).then_inc(dots_spread, 1)
                act.wait_ge(turned_ready, batch + 1)
                if not first:
                    act.wait_ge(scale_ready, batch * TB)
                nc.scalar.activation(growth[:], turned[:], ACT.Identity,
                                     bias=ones[:, 0:1]).then_inc(growth_ready, 1)

            def store(batch, half, round_):
                for t in range(TB):
                    s = half * TB + t
                    act.wait_ge(tiles_done, batch * TB + t + 1)
                    act.dma_start(out[bass.ds((round_ * n_slots + s) * P, P), :],
                                  tiles[:, s, :]).then_inc(y_stored[s], 16)

            make_growth(0, first=True)
            store(0, 0, 0)
            make_growth(1)
            with act.Fori(1, n_rounds) as r:
                store(r * 2 - 1, 1, r - 1)
                make_growth(r * 2)
                store(r * 2, 0, r)
                make_growth(r * 2 + 1)
            store(n_batches - 1, 1, n_rounds - 1)
            for s in range(n_slots):
                act.wait_ge(y_stored[s], 16 * n_rounds)

        @block.vector
        def _(dve):
            nc.vector.memset(w_stage[:, D // 2:D], 0.0).then_inc(stage_zeroed, 1)
            nc.vector.memset(ones[:], 1.0).then_inc(ones_ready, 1)
            for g in range(G):
                dve.wait_ge(w_landed[g], 16)
            dve.wait_ge(stage_zeroed, 2)
            nc.vector.transpose(weights[:].rearrange("p k q -> p (k q)"), w_stage).then_inc(weights_ready, 1)

            for h in range(n_halves):
                dve.wait_ge(scratch_filled, h + 1)
                at = slice(h * HALF, (h + 1) * HALF)
                nc.vector.tensor_tensor_reduce(out=cw_prod[:, at], in0=scratch[0:L, :], in1=w_stage[0:L, at],
                                               scale=1.0, scalar=0.0, op0=ALU.mult, op1=ALU.add,
                                               accum_out=cw_part[:, h:h + 1]).then_inc(products_summed, 1)
            dve.wait_ge(products_summed, n_halves)
            nc.vector.reduce_sum(cw_sum[:], cw_part[:], mybir.AxisListType.X).then_inc(cw_summed, 1)
            dve.wait_ge(cw_summed, 1)
            dve.wait_ge(masks_built, 4 + P // LP)
            nc.vector.tensor_scalar(cw_diag[:], ident[:], cw_sum[:, 0:1], None, ALU.mult).then_inc(cw_diag_ready, 1)
            nc.vector.reduce_sum(group_mask[:], lanes[:].rearrange("p (i g) -> p g i", g=G),
                                 mybir.AxisListType.X).then_inc(group_mask_ready, 1)

            def transpose_chunk(chunk, c, half):
                nc.vector.transpose(blocks[:, c % 2, :, :].rearrange("p t n -> p (t n)"),
                                    tiles[:, half * TB:(half + 1) * TB, c * CH:(c + 1) * CH]
                                    ).then_inc(blocks_ready, 1)

            def scan(batch, half):
                dve.wait_ge(growth_ready, batch + 1)
                for t in range(TB):
                    nc.vector.tensor_tensor_scan(scale[:, half, t, 0:L], growth[:, t, 0:L], cw[:, 0:L],
                                                 1.0, ALU.mult, ALU.add).then_inc(scale_ready, 1)

            def finish(batch, half, t):
                s = half * TB + t
                dve.wait_ge(scale_ready, batch * TB + t + 1)
                nc.vector.scalar_tensor_tensor(out=tiles[:, s, :], in0=tiles[:, s, :],
                                               scalar=scale[:, half, t, L - 1:L], in1=c_last[:],
                                               op0=ALU.mult, op1=ALU.add).then_inc(tiles_done, 1)

            def transpose_and_finish(batch, half, landed):
                for s in range(half * TB, (half + 1) * TB):
                    dve.wait_ge(x_landed[s], landed)
                for c in range(NCHUNK):
                    dve.wait_ge(blocks_used, batch * NCHUNK + c - 1)
                    transpose_chunk(batch * NCHUNK + c, c, half)
                    if c == 1:
                        scan(batch - 1, 1 - half)
                    if c >= 1:
                        finish(batch - 1, 1 - half, c - 1)
                finish(batch - 1, 1 - half, TB - 1)

            for c in range(NCHUNK):
                if c >= 2:
                    dve.wait_ge(blocks_used, c - 1)
                for t in range(TB):
                    dve.wait_ge(x_landed[t], 16)
                    last = nc.vector.transpose(blocks[:, c % 2, t, :], tiles[:, t, c * CH:(c + 1) * CH])
                last.then_inc(blocks_ready, 1)
            dve.wait_ge(scratch_copied, n_halves + 1)
            transpose_and_finish(1, 1, 16)
            with dve.Fori(1, n_rounds) as r:
                transpose_and_finish(r * 2, 0, r * 16 + 16)
                transpose_and_finish(r * 2 + 1, 1, r * 16 + 16)
            scan(n_batches - 1, 1)
            for t in range(TB):
                finish(n_batches - 1, 1, t)

        @block.tensor
        def _(pe):
            pe.wait_ge(b_landed, 16)
            pe.wait_ge(ones_ready, 1)
            pe.wait_ge(masks_built, 2)
            for h in range(2 * n_halves):
                if h >= 1 and h <= n_halves:
                    pe.wait_ge(products_summed, h)
                if h > n_halves:
                    pe.wait_ge(scratch_copied, h - n_halves)
                for c in range(HALF_BANKS):
                    at = (h % n_halves) * HALF + c * BANK
                    into = scratch[:, c * BANK:(c + 1) * BANK]
                    if h < n_halves:
                        last = nc.tensor.matmul(into[0:L, :], earlier[:, 0:L], b_stage[:, at:at + BANK],
                                                start=True, stop=True)
                    else:
                        last = nc.tensor.matmul(into, ones[0:L, :], b_stage[:, at:at + BANK],
                                                start=True, stop=True)
                last.then_inc(scratch_filled, 1)
            pe.wait_ge(scratch_copied, n_halves)
            pe.wait_ge(cw_diag_ready, 1)
            nc.tensor.matmul(scratch[:, 0:LP], ones[0:L, :], cw_diag[:], start=True,
                             stop=True).then_inc(scratch_filled, 1)
            pe.wait_ge(weights_ready, 1)

            def batch_dots(batch, first=False):
                if not first:
                    pe.wait_ge(dots_spread, batch * G)
                for c in range(NCHUNK):
                    pe.wait_ge(blocks_ready, batch * NCHUNK + c + 1)
                    for k in range(KB):
                        i = k % G
                        last = nc.tensor.matmul(dots[i * Q:(i + 1) * Q, :, :],
                                                weights[:, c * KB + k, :],
                                                blocks[:, c % 2, :, k * Q:(k + 1) * Q],
                                                start=(c == 0 and k < G), stop=(c == NCHUNK - 1 and k >= KB - G),
                                                tile_position=(0, i * Q))
                    last.then_inc(blocks_used, 1)
                pe.wait_ge(dots_spread, batch * G + G)
                if not first:
                    pe.wait_ge(growth_ready, batch)
                else:
                    pe.wait_ge(masks_built, 4 + P // LP)
                for t in range(TB):
                    last = nc.tensor.matmul(turned[:, t, :], spread[:, t, :, :].rearrange("p g q -> p (g q)"),
                                            layer_sel[:], start=True, stop=True)
                last.then_inc(turned_ready, 1)

            batch_dots(0, first=True)
            with pe.Fori(1, n_batches) as n:
                batch_dots(n)


_INS = ["r_inputs", "L0_rec_w", "L0_rec_b"]


def kernel(**inputs):
    import numpy as _np
    import concourse.bacc as _bacc
    from concourse import mybir as _mybir
    from concourse.bass_utils import run_bass_kernel_spmd as _run

    nc = _bacc.Bacc("TRN2", target_bir_lowering=False, num_devices=1)
    arrays, args = {}, []
    for name in _INS:
        a = _np.ascontiguousarray(inputs[name])
        arrays[f"in_{name}_dram"] = a
        args.append(nc.dram_tensor(f"in_{name}_dram", a.shape, _mybir.dt.from_np(a.dtype), kind="ExternalInput").ap())
    shape = tuple(arrays["in_r_inputs_dram"].shape)
    out = nc.dram_tensor("out_0_dram", shape, _mybir.dt.float32, kind="ExternalOutput").ap()
    cross_network(nc, *args, out)
    r = _run(nc, [arrays], core_ids=[0])
    return r.results[0]["out_0_dram"]
```

```python
from contextlib import ExitStack

import concourse.bass as bass
from concourse import mybir

F32 = mybir.dt.float32
ALU = mybir.AluOpType
ACT = mybir.ActivationFunctionType

P = 128
Q = 32
G = P // Q
TB = 2
BR = 4
KM = 2
NCHUNK = 4
LP = 8
BANK = 512
HALF_BANKS = 4


def cross_network(nc, x, w, b, out):
    rows, D = x.shape
    L = w.shape[0]
    n_tiles = rows // P
    n_batches = n_tiles // TB
    n_slots = BR * TB
    n_rounds = n_batches // BR
    CH = D // NCHUNK
    KB = CH // Q
    HALF = HALF_BANKS * BANK
    n_halves = D // HALF
    assert L <= LP and G * LP == Q and n_tiles % n_slots == 0 and D % HALF == 0 and CH % (Q * G) == 0

    w_rows = w.rearrange("l d a -> l (d a)")

    with ExitStack() as ctx:
        def sb(name, shape):
            return ctx.enter_context(nc.sbuf_tensor(name, shape, F32))

        def ps(name, shape):
            return ctx.enter_context(nc.psum_tensor(name, shape, F32))

        def sem(name):
            return ctx.enter_context(nc.semaphore(name))

        tiles = sb("tiles", [P, n_slots, D])
        blocks = sb("blocks", [P, NCHUNK, TB, CH])
        weights = sb("weights", [P, D // Q, Q])
        c_last = sb("c_last", [P, D])
        ones = sb("ones", [P, P])
        earlier = sb("earlier", [L, LP])
        ident = sb("ident", [L, LP])
        group_mask = sb("group_mask", [P, G])
        lanes = sb("lanes", [P, P // LP])
        layer_sel = sb("layer_sel", [P, KM, LP])
        cw_part = sb("cw_part", [L, n_halves])
        cw_sum = sb("cw_sum", [L, 1])
        cw_diag = sb("cw_diag", [L, LP])
        cw = sb("cw", [P, LP])
        spread = sb("spread", [P, TB, KM, G, Q])
        growth = sb("growth", [P, TB, LP])
        scale = sb("scale", [P, 2, TB, LP])

        w_stage = tiles[:, n_slots - 1, :]
        b_stage = tiles[0:L, n_slots - 2, :]
        cw_prod = tiles[0:L, n_slots - 3, :]

        dots = ps("dots", [P, TB, KM, Q])
        turned = ps("turned", [P, TB, LP])
        scratch = ps("scratch", [P, HALF])

        x_landed = [sem(f"x_landed{s}") for s in range(n_slots)]
        y_stored = [sem(f"y_stored{s}") for s in range(n_slots)]
        w_landed = [sem(f"w_landed{g}") for g in range(G)]
        b_landed = sem("b_landed")
        stage_zeroed = sem("stage_zeroed")
        ones_ready = sem("ones_ready")
        zeros_ready = sem("zeros_ready")
        masks_built = sem("masks_built")
        weights_ready = sem("weights_ready")
        group_mask_ready = sem("group_mask_ready")
        scratch_filled = sem("scratch_filled")
        products_summed = sem("products_summed")
        cw_summed = sem("cw_summed")
        cw_diag_ready = sem("cw_diag_ready")
        scratch_copied = sem("scratch_copied")
        blocks_ready = sem("blocks_ready")
        blocks_used = sem("blocks_used")
        dots_spread = sem("dots_spread")
        turned_ready = sem("turned_ready")
        growth_ready = sem("growth_ready")
        scale_ready = sem("scale_ready")
        tiles_done = sem("tiles_done")

        block = ctx.enter_context(nc.Block())

        @block.sync
        def _(sp):
            for s in range(n_slots):
                if s == n_slots - 3:
                    sp.wait_ge(products_summed, n_halves)
                    sp.wait_ge(scratch_filled, 2 * n_halves)
                    sp.wait_ge(weights_ready, 1)
                sp.dma_start(tiles[:, s, :], x[s * P:(s + 1) * P, :]).then_inc(x_landed[s], 16)
            with sp.Fori(1, n_rounds) as r:
                for s in range(n_slots):
                    sp.wait_ge(y_stored[s], r * 16)
                    sp.dma_start(tiles[:, s, :], x[bass.ds((r * n_slots + s) * P, P), :]).then_inc(x_landed[s], 16)

        @block.gpsimd
        def _(pool):
            nc.gpsimd.memset(w_stage[:, 0:D // 2], 0.0).then_inc(stage_zeroed, 1)
            nc.gpsimd.memset(layer_sel[:], 0.0).then_inc(zeros_ready, 1)
            nc.gpsimd.memset(ident[:], 0.0).then_inc(zeros_ready, 1)
            pool.wait_ge(ones_ready, 1)
            nc.gpsimd.affine_select(out=earlier[:], in_=ones[0:L, 0:LP], compare_op=ALU.is_ge, fill=0.0,
                                    base=-1, pattern=[[1, LP]], channel_multiplier=-1).then_inc(masks_built, 1)
            pool.wait_ge(zeros_ready, 2)
            nc.gpsimd.affine_select(out=ident[:], in_=ident[:], compare_op=ALU.not_equal, fill=1.0,
                                    base=0, pattern=[[-1, LP]], channel_multiplier=1).then_inc(masks_built, 1)
            for q in range(P // LP):
                m = q // G % KM
                nc.gpsimd.affine_select(out=layer_sel[:, m, :], in_=layer_sel[:, m, :],
                                        compare_op=ALU.not_equal, fill=1.0,
                                        base=-q * LP, pattern=[[-1, LP]],
                                        channel_multiplier=1).then_inc(masks_built, 1)
                pool.wait_ge(masks_built, 3 + q)
            nc.gpsimd.affine_select(out=lanes[:], in_=ones[:, 0:P // LP], compare_op=ALU.is_ge, fill=0.0,
                                    base=0, pattern=[[-LP, P // LP]],
                                    channel_multiplier=1).then_inc(masks_built, 1)
            pool.wait_ge(masks_built, 3 + P // LP)
            nc.gpsimd.affine_select(out=lanes[:], in_=lanes[:], compare_op=ALU.is_ge, fill=0.0,
                                    base=LP - 1, pattern=[[LP, P // LP]],
                                    channel_multiplier=-1).then_inc(masks_built, 1)

        @block.scalar
        def _(act):
            act.dma_start(b_stage, b).then_inc(b_landed, 16)
            act.wait_ge(stage_zeroed, 2)
            for g in range(G):
                at = g * Q + g * LP
                act.dma_start(w_stage[at:at + L, :], w_rows).then_inc(w_landed[g], 16)
            for h in range(n_halves):
                act.wait_ge(scratch_filled, n_halves + h + 1)
                nc.scalar.copy(c_last[:, h * HALF:(h + 1) * HALF], scratch[:]).then_inc(scratch_copied, 1)
            act.wait_ge(scratch_filled, 2 * n_halves + 1)
            nc.scalar.copy(cw[:], scratch[:, 0:LP]).then_inc(scratch_copied, 1)

            def make_growth(batch, first=False):
                act.wait_ge(blocks_used, (batch + 1) * NCHUNK)
                if first:
                    act.wait_ge(group_mask_ready, 1)
                for g in range(G):
                    nc.scalar.activation(spread[:, :, :, g, :], dots[:], ACT.Copy,
                                         scale=group_mask[:, g:g + 1]).then_inc(dots_spread, 1)
                act.wait_ge(turned_ready, batch + 1)
                if not first:
                    act.wait_ge(scale_ready, batch * TB)
                nc.scalar.activation(growth[:], turned[:], ACT.Identity,
                                     bias=ones[:, 0:1]).then_inc(growth_ready, 1)

            def store(batch, round_, q):
                for t in range(TB):
                    s = q * TB + t
                    act.wait_ge(tiles_done, batch * TB + t + 1)
                    act.dma_start(out[bass.ds((round_ * n_slots + s) * P, P), :],
                                  tiles[:, s, :]).then_inc(y_stored[s], 16)

            make_growth(0, first=True)
            for q in range(1, BR):
                store(q - 1, 0, q - 1)
                make_growth(q)
            with act.Fori(1, n_rounds) as r:
                store(r * BR - 1, r - 1, BR - 1)
                make_growth(r * BR)
                for q in range(1, BR):
                    store(r * BR + q - 1, r, q - 1)
                    make_growth(r * BR + q)
            store(n_batches - 1, n_rounds - 1, BR - 1)
            for s in range(n_slots):
                act.wait_ge(y_stored[s], 16 * n_rounds)

        @block.vector
        def _(dve):
            nc.vector.memset(w_stage[:, D // 2:D], 0.0).then_inc(stage_zeroed, 1)
            nc.vector.memset(ones[:], 1.0).then_inc(ones_ready, 1)
            for g in range(G):
                dve.wait_ge(w_landed[g], 16)
            dve.wait_ge(stage_zeroed, 2)
            nc.vector.transpose(weights[:].rearrange("p k q -> p (k q)"), w_stage).then_inc(weights_ready, 1)

            for h in range(n_halves):
                dve.wait_ge(scratch_filled, h + 1)
                at = slice(h * HALF, (h + 1) * HALF)
                nc.vector.tensor_tensor_reduce(out=cw_prod[:, at], in0=scratch[0:L, :], in1=w_stage[0:L, at],
                                               scale=1.0, scalar=0.0, op0=ALU.mult, op1=ALU.add,
                                               accum_out=cw_part[:, h:h + 1]).then_inc(products_summed, 1)
            dve.wait_ge(products_summed, n_halves)
            nc.vector.reduce_sum(cw_sum[:], cw_part[:], mybir.AxisListType.X).then_inc(cw_summed, 1)
            dve.wait_ge(cw_summed, 1)
            dve.wait_ge(masks_built, 4 + P // LP)
            nc.vector.tensor_scalar(cw_diag[:], ident[:], cw_sum[:, 0:1], None, ALU.mult).then_inc(cw_diag_ready, 1)
            nc.vector.reduce_sum(group_mask[:], lanes[:].rearrange("p (i g) -> p g i", g=G),
                                 mybir.AxisListType.X).then_inc(group_mask_ready, 1)

            def transpose_chunk(batch, q, c):
                nc.vector.transpose(blocks[:, c, :, :].rearrange("p t n -> p (t n)"),
                                    tiles[:, q * TB:(q + 1) * TB, c * CH:(c + 1) * CH]
                                    ).then_inc(blocks_ready, 1)

            def scan(batch, q):
                dve.wait_ge(growth_ready, batch + 1)
                for t in range(TB):
                    nc.vector.tensor_tensor_scan(scale[:, q % 2, t, 0:L], growth[:, t, 0:L], cw[:, 0:L],
                                                 1.0, ALU.mult, ALU.add).then_inc(scale_ready, 1)

            def finish(batch, q, t):
                s = q * TB + t
                dve.wait_ge(scale_ready, batch * TB + t + 1)
                nc.vector.scalar_tensor_tensor(out=tiles[:, s, :], in0=tiles[:, s, :],
                                               scalar=scale[:, q % 2, t, L - 1:L], in1=c_last[:],
                                               op0=ALU.mult, op1=ALU.add).then_inc(tiles_done, 1)

            def transpose_and_finish(batch, q, landed):
                for s in range(q * TB, (q + 1) * TB):
                    dve.wait_ge(x_landed[s], landed)
                for c in range(NCHUNK):
                    dve.wait_ge(blocks_used, (batch - 1) * NCHUNK + c + 1)
                    transpose_chunk(batch, q, c)
                    if c == 1:
                        scan(batch - 1, (q - 1) % BR)
                    if c % 2 == 1:
                        finish(batch - 1, (q - 1) % BR, c // 2)

            for t in range(TB):
                dve.wait_ge(x_landed[t], 16)
                for c in range(NCHUNK):
                    last = nc.vector.transpose(blocks[:, c, t, :], tiles[:, t, c * CH:(c + 1) * CH])
                    if t == TB - 1:
                        last.then_inc(blocks_ready, 1)
            dve.wait_ge(scratch_copied, n_halves + 1)
            for q in range(1, BR):
                transpose_and_finish(q, q, 16)
            with dve.Fori(1, n_rounds) as r:
                for q in range(BR):
                    transpose_and_finish(r * BR + q, q, r * 16 + 16)
            scan(n_batches - 1, BR - 1)
            for t in range(TB):
                finish(n_batches - 1, BR - 1, t)

        @block.tensor
        def _(pe):
            pe.wait_ge(b_landed, 16)
            pe.wait_ge(ones_ready, 1)
            pe.wait_ge(masks_built, 2)
            for h in range(2 * n_halves):
                if h >= 1 and h <= n_halves:
                    pe.wait_ge(products_summed, h)
                if h > n_halves:
                    pe.wait_ge(scratch_copied, h - n_halves)
                for c in range(HALF_BANKS):
                    at = (h % n_halves) * HALF + c * BANK
                    into = scratch[:, c * BANK:(c + 1) * BANK]
                    if h < n_halves:
                        last = nc.tensor.matmul(into[0:L, :], earlier[:, 0:L], b_stage[:, at:at + BANK],
                                                start=True, stop=True)
                    else:
                        last = nc.tensor.matmul(into, ones[0:L, :], b_stage[:, at:at + BANK],
                                                start=True, stop=True)
                last.then_inc(scratch_filled, 1)
            pe.wait_ge(scratch_copied, n_halves)
            pe.wait_ge(cw_diag_ready, 1)
            nc.tensor.matmul(scratch[:, 0:LP], ones[0:L, :], cw_diag[:], start=True,
                             stop=True).then_inc(scratch_filled, 1)
            pe.wait_ge(weights_ready, 1)

            parts = G // KM

            def batch_dots(batch, first=False):
                if not first:
                    pe.wait_ge(dots_spread, batch * G)
                for c in range(NCHUNK):
                    pe.wait_ge(blocks_ready, batch * NCHUNK + c + 1)
                    for k in range(0, KB, KM):
                        i = k // KM % parts
                        at = i * KM * Q
                        last = nc.tensor.matmul(dots[at:at + KM * Q, :, :, :],
                                                weights[:, c * KB + k:c * KB + k + KM, :],
                                                blocks[:, c, :, k * Q:(k + KM) * Q],
                                                start=(c == 0 and k < parts * KM),
                                                stop=(c == NCHUNK - 1 and k >= KB - parts * KM),
                                                tile_position=(0, at))
                    last.then_inc(blocks_used, 1)
                pe.wait_ge(dots_spread, batch * G + G)
                if not first:
                    pe.wait_ge(growth_ready, batch)
                else:
                    pe.wait_ge(masks_built, 4 + P // LP)
                for t in range(TB):
                    for m in range(KM):
                        last = nc.tensor.matmul(turned[:, t, :], spread[:, t, m, :, :], layer_sel[:, m, :],
                                                start=(m == 0), stop=(m == KM - 1))
                last.then_inc(turned_ready, 1)

            batch_dots(0, first=True)
            with pe.Fori(1, n_batches) as n:
                batch_dots(n)


_INS = ["r_inputs", "L0_rec_w", "L0_rec_b"]


def kernel(**inputs):
    import numpy as _np
    import concourse.bacc as _bacc
    from concourse import mybir as _mybir
    from concourse.bass_utils import run_bass_kernel_spmd as _run

    nc = _bacc.Bacc("TRN2", target_bir_lowering=False, num_devices=1)
    arrays, args = {}, []
    for name in _INS:
        a = _np.ascontiguousarray(inputs[name])
        arrays[f"in_{name}_dram"] = a
        args.append(nc.dram_tensor(f"in_{name}_dram", a.shape, _mybir.dt.from_np(a.dtype), kind="ExternalInput").ap())
    shape = tuple(arrays["in_r_inputs_dram"].shape)
    out = nc.dram_tensor("out_0_dram", shape, _mybir.dt.float32, kind="ExternalOutput").ap()
    cross_network(nc, *args, out)
    r = _run(nc, [arrays], core_ids=[0])
    return r.results[0]["out_0_dram"]
```

```python
from contextlib import ExitStack

import concourse.bass as bass
from concourse import mybir

F32 = mybir.dt.float32
ALU = mybir.AluOpType
ACT = mybir.ActivationFunctionType

P = 128
Q = 32
G = P // Q
TB = 2
BR = 4
KM = 2
NCHUNK = 4
LP = 8
BANK = 512
HALF_BANKS = 4
S = 16
PIECES = 4


def cross_network(nc, x, w, b, out):
    rows, D = x.shape
    L = w.shape[0]
    n_tiles = rows // P
    n_batches = n_tiles // TB
    n_slots = BR * TB
    n_rounds = n_batches // BR
    CH = D // NCHUNK
    KB = CH // Q
    HALF = HALF_BANKS * BANK
    n_halves = D // HALF
    assert L <= LP and G * LP == Q and n_tiles % n_slots == 0 and D % HALF == 0 and CH % (Q * G) == 0

    SW = D // S
    PW = D // PIECES
    w_rows = w.rearrange("l d a -> l (d a)")
    w_strips = w.rearrange("l (s n) a -> (l s) (n a)", s=S)
    b_strips = b.rearrange("l (s n) -> (l s) n", s=S)

    with ExitStack() as ctx:
        def sb(name, shape):
            return ctx.enter_context(nc.sbuf_tensor(name, shape, F32))

        def ps(name, shape):
            return ctx.enter_context(nc.psum_tensor(name, shape, F32))

        def sem(name):
            return ctx.enter_context(nc.semaphore(name))

        tiles = sb("tiles", [P, n_slots, D])
        blocks = sb("blocks", [P, NCHUNK, TB, CH])
        weights = sb("weights", [P, D // Q, Q])
        c_last = sb("c_last", [P, D])
        ones = sb("ones", [P, P])
        strips_w = sb("strips_w", [L * S, SW])
        strips_b = sb("strips_b", [L * S, SW])
        earlier = sb("earlier", [L * S, L * S])
        of_layer = sb("of_layer", [L * S, LP])
        cw_part = sb("cw_part", [L * S, 1])
        cw_diag = sb("cw_diag", [L * S, LP])
        cw = sb("cw", [P, LP])
        group_mask = sb("group_mask", [P, G])
        lanes = sb("lanes", [P, P // LP])
        layer_sel = sb("layer_sel", [P, KM, LP])
        spread = sb("spread", [P, TB, KM, G, Q])
        growth = sb("growth", [P, TB, LP])
        scale = sb("scale", [P, 2, TB, LP])

        w_stage = tiles[:, n_slots - 1, :]
        b_stage = tiles[0:L, n_slots - 2, :]

        dots = ps("dots", [P, TB, KM, Q])
        turned = ps("turned", [P, TB, LP])
        scratch = ps("scratch", [P, HALF])
        strips_c = ps("strips_c", [L * S, SW])
        cw_all = ps("cw_all", [P, LP])

        x_landed = [sem(f"x_landed{s}") for s in range(n_slots)]
        y_stored = [sem(f"y_stored{s}") for s in range(n_slots)]
        w_landed = [sem(f"w_landed{g}") for g in range(G)]
        b_landed = sem("b_landed")
        strips_w_landed = sem("strips_w_landed")
        strips_b_landed = sem("strips_b_landed")
        stage_zeroed = sem("stage_zeroed")
        ones_ready = sem("ones_ready")
        zeros_ready = sem("zeros_ready")
        masks_built = sem("masks_built")
        weights_ready = sem("weights_ready")
        group_mask_ready = sem("group_mask_ready")
        strips_c_ready = sem("strips_c_ready")
        strips_summed = sem("strips_summed")
        cw_diag_ready = sem("cw_diag_ready")
        cw_all_ready = sem("cw_all_ready")
        cw_ready = sem("cw_ready")
        scratch_filled = sem("scratch_filled")
        scratch_copied = sem("scratch_copied")
        blocks_ready = sem("blocks_ready")
        blocks_used = sem("blocks_used")
        dots_spread = sem("dots_spread")
        turned_ready = sem("turned_ready")
        growth_ready = sem("growth_ready")
        scale_ready = sem("scale_ready")
        tiles_done = sem("tiles_done")

        block = ctx.enter_context(nc.Block())

        @block.sync
        def _(sp):
            sp.dma_start(strips_b[:], b_strips).then_inc(strips_b_landed, 16)
            sp.dma_start(strips_w[:], w_strips).then_inc(strips_w_landed, 16)
            sp.dma_start(b_stage, b).then_inc(b_landed, 16)
            sp.dma_start(tiles[:, 0, :], x[0:P, :]).then_inc(x_landed[0], 16)
            sp.wait_ge(stage_zeroed, 2)
            for g in range(G):
                at = g * Q + g * LP
                sp.dma_start(w_stage[at:at + L, :], w_rows).then_inc(w_landed[g], 16)
            for s in range(1, n_slots):
                if s == n_slots - 2:
                    sp.wait_ge(scratch_filled, n_halves)
                    sp.wait_ge(weights_ready, 1)
                sp.dma_start(tiles[:, s, :], x[s * P:(s + 1) * P, :]).then_inc(x_landed[s], 16)
            with sp.Fori(1, n_rounds) as r:
                for s in range(n_slots):
                    sp.wait_ge(y_stored[s], r * 16)
                    sp.dma_start(tiles[:, s, :], x[bass.ds((r * n_slots + s) * P, P), :]).then_inc(x_landed[s], 16)

        @block.gpsimd
        def _(pool):
            nc.gpsimd.memset(w_stage[:, 0:D // 2], 0.0).then_inc(stage_zeroed, 1)
            nc.gpsimd.memset(layer_sel[:], 0.0).then_inc(zeros_ready, 1)
            nc.gpsimd.memset(earlier[:], 0.0).then_inc(zeros_ready, 1)
            for d in range(1, L):
                pool.wait_ge(zeros_ready, 1 + d)
                nc.gpsimd.affine_select(out=earlier[:], in_=earlier[:], compare_op=ALU.not_equal, fill=1.0,
                                        base=d * S, pattern=[[-1, L * S]],
                                        channel_multiplier=1).then_inc(zeros_ready, 1)
            pool.wait_ge(ones_ready, 1)
            nc.gpsimd.affine_select(out=of_layer[:], in_=ones[0:L * S, 0:LP], compare_op=ALU.is_ge, fill=0.0,
                                    base=0, pattern=[[-S, LP]], channel_multiplier=1).then_inc(masks_built, 1)
            pool.wait_ge(masks_built, 1)
            nc.gpsimd.affine_select(out=of_layer[:], in_=of_layer[:], compare_op=ALU.is_ge, fill=0.0,
                                    base=S - 1, pattern=[[S, LP]], channel_multiplier=-1).then_inc(masks_built, 1)
            for q in range(P // LP):
                m = q // G % KM
                nc.gpsimd.affine_select(out=layer_sel[:, m, :], in_=layer_sel[:, m, :],
                                        compare_op=ALU.not_equal, fill=1.0,
                                        base=-q * LP, pattern=[[-1, LP]],
                                        channel_multiplier=1).then_inc(masks_built, 1)
                pool.wait_ge(masks_built, 3 + q)
            nc.gpsimd.affine_select(out=lanes[:], in_=ones[:, 0:P // LP], compare_op=ALU.is_ge, fill=0.0,
                                    base=0, pattern=[[-LP, P // LP]],
                                    channel_multiplier=1).then_inc(masks_built, 1)
            pool.wait_ge(masks_built, 3 + P // LP)
            nc.gpsimd.affine_select(out=lanes[:], in_=lanes[:], compare_op=ALU.is_ge, fill=0.0,
                                    base=LP - 1, pattern=[[LP, P // LP]],
                                    channel_multiplier=-1).then_inc(masks_built, 1)

        @block.scalar
        def _(act):
            for h in range(n_halves):
                act.wait_ge(scratch_filled, h + 1)
                nc.scalar.copy(c_last[:, h * HALF:(h + 1) * HALF], scratch[:]).then_inc(scratch_copied, 1)
            act.wait_ge(cw_all_ready, 1)
            nc.scalar.copy(cw[:], cw_all[:]).then_inc(cw_ready, 1)

            def make_growth(batch, first=False):
                act.wait_ge(blocks_used, (batch + 1) * NCHUNK)
                if first:
                    act.wait_ge(group_mask_ready, 1)
                for g in range(G):
                    nc.scalar.activation(spread[:, :, :, g, :], dots[:], ACT.Copy,
                                         scale=group_mask[:, g:g + 1]).then_inc(dots_spread, 1)
                act.wait_ge(turned_ready, batch + 1)
                if not first:
                    act.wait_ge(scale_ready, batch * TB)
                nc.scalar.activation(growth[:], turned[:], ACT.Identity,
                                     bias=ones[:, 0:1]).then_inc(growth_ready, 1)

            def store(batch, round_, q):
                for t in range(TB):
                    s = q * TB + t
                    act.wait_ge(tiles_done, batch * TB + t + 1)
                    act.dma_start(out[bass.ds((round_ * n_slots + s) * P, P), :],
                                  tiles[:, s, :]).then_inc(y_stored[s], 16)

            make_growth(0, first=True)
            for q in range(1, BR):
                store(q - 1, 0, q - 1)
                make_growth(q)
            with act.Fori(1, n_rounds) as r:
                store(r * BR - 1, r - 1, BR - 1)
                make_growth(r * BR)
                for q in range(1, BR):
                    store(r * BR + q - 1, r, q - 1)
                    make_growth(r * BR + q)
            for n in range(TB * PIECES):
                s = n_slots - TB + n // PIECES
                at = slice(n % PIECES * PW, (n % PIECES + 1) * PW)
                act.wait_ge(tiles_done, n_tiles - TB + n + 1)
                act.dma_start(out[(n_tiles - n_slots + s) * P:(n_tiles - n_slots + s + 1) * P, at],
                              tiles[:, s, at]).then_inc(y_stored[s], 16)
            for s in range(n_slots):
                last_stores = 1 if s < n_slots - TB else PIECES
                act.wait_ge(y_stored[s], 16 * (n_rounds - 1 + last_stores))

        @block.vector
        def _(dve):
            nc.vector.memset(w_stage[:, D // 2:D], 0.0).then_inc(stage_zeroed, 1)
            nc.vector.memset(ones[:], 1.0).then_inc(ones_ready, 1)

            def transpose_tile(t):
                dve.wait_ge(x_landed[t], 16)
                for c in range(NCHUNK):
                    last = nc.vector.transpose(blocks[:, c, t, :], tiles[:, t, c * CH:(c + 1) * CH])
                    if t == TB - 1:
                        last.then_inc(blocks_ready, 1)

            transpose_tile(0)
            for g in range(G):
                dve.wait_ge(w_landed[g], 16)
            dve.wait_ge(stage_zeroed, 2)
            nc.vector.transpose(weights[:].rearrange("p k q -> p (k q)"), w_stage).then_inc(weights_ready, 1)
            dve.wait_ge(strips_w_landed, 16)
            dve.wait_ge(strips_c_ready, 1)
            nc.vector.tensor_tensor_reduce(out=strips_w[:], in0=strips_c[:], in1=strips_w[:],
                                           scale=1.0, scalar=0.0, op0=ALU.mult, op1=ALU.add,
                                           accum_out=cw_part[:]).then_inc(strips_summed, 1)
            dve.wait_ge(strips_summed, 1)
            dve.wait_ge(masks_built, 4 + P // LP)
            nc.vector.tensor_scalar(cw_diag[:], of_layer[:], cw_part[:, 0:1], None, ALU.mult).then_inc(cw_diag_ready, 1)
            nc.vector.reduce_sum(group_mask[:], lanes[:].rearrange("p (i g) -> p g i", g=G),
                                 mybir.AxisListType.X).then_inc(group_mask_ready, 1)
            for t in range(1, TB):
                transpose_tile(t)

            def transpose_chunk(batch, q, c):
                nc.vector.transpose(blocks[:, c, :, :].rearrange("p t n -> p (t n)"),
                                    tiles[:, q * TB:(q + 1) * TB, c * CH:(c + 1) * CH]
                                    ).then_inc(blocks_ready, 1)

            def scan(batch, q):
                dve.wait_ge(growth_ready, batch + 1)
                for t in range(TB):
                    nc.vector.tensor_tensor_scan(scale[:, q % 2, t, 0:L], growth[:, t, 0:L], cw[:, 0:L],
                                                 1.0, ALU.mult, ALU.add).then_inc(scale_ready, 1)

            def finish(batch, q, t):
                s = q * TB + t
                dve.wait_ge(scale_ready, batch * TB + t + 1)
                nc.vector.scalar_tensor_tensor(out=tiles[:, s, :], in0=tiles[:, s, :],
                                               scalar=scale[:, q % 2, t, L - 1:L], in1=c_last[:],
                                               op0=ALU.mult, op1=ALU.add).then_inc(tiles_done, 1)

            def transpose_and_finish(batch, q, landed, last=False):
                for s in range(q * TB, (q + 1) * TB):
                    dve.wait_ge(x_landed[s], landed)
                for c in range(NCHUNK):
                    dve.wait_ge(blocks_used, (batch - 1) * NCHUNK + c + 1)
                    transpose_chunk(batch, q, c)
                finish(batch - 1, (q - 1) % BR, TB - 1)
                scan(batch, q)
                for t in range(0 if last else TB - 1):
                    finish(batch, q, t)

            dve.wait_ge(scratch_copied, n_halves)
            dve.wait_ge(cw_ready, 1)
            scan(0, 0)
            for t in range(TB - 1):
                finish(0, 0, t)
            for q in range(1, BR):
                transpose_and_finish(q, q, 16)
            with dve.Fori(1, n_rounds - 1) as r:
                for q in range(BR):
                    transpose_and_finish(r * BR + q, q, r * 16 + 16)
            for q in range(BR):
                transpose_and_finish((n_rounds - 1) * BR + q, q, n_rounds * 16, last=(q == BR - 1))
            dve.wait_ge(scale_ready, n_tiles)
            for n in range(TB * PIECES):
                t = n // PIECES
                s = n_slots - TB + t
                at = slice(n % PIECES * PW, (n % PIECES + 1) * PW)
                nc.vector.scalar_tensor_tensor(out=tiles[:, s, at], in0=tiles[:, s, at],
                                               scalar=scale[:, (BR - 1) % 2, t, L - 1:L], in1=c_last[:, at],
                                               op0=ALU.mult, op1=ALU.add).then_inc(tiles_done, 1)

        @block.tensor
        def _(pe):
            pe.wait_ge(strips_b_landed, 16)
            pe.wait_ge(zeros_ready, 1 + L)
            nc.tensor.matmul(strips_c[:], earlier[:], strips_b[:], start=True, stop=True).then_inc(strips_c_ready, 1)
            pe.wait_ge(b_landed, 16)
            pe.wait_ge(ones_ready, 1)
            for h in range(n_halves):
                if h >= 1:
                    pe.wait_ge(scratch_copied, h)
                for c in range(HALF_BANKS):
                    at = h * HALF + c * BANK
                    last = nc.tensor.matmul(scratch[:, c * BANK:(c + 1) * BANK], ones[0:L, :],
                                            b_stage[:, at:at + BANK], start=True, stop=True)
                last.then_inc(scratch_filled, 1)
            pe.wait_ge(cw_diag_ready, 1)
            nc.tensor.matmul(cw_all[:], ones[0:L * S, :], cw_diag[:], start=True, stop=True).then_inc(cw_all_ready, 1)
            pe.wait_ge(weights_ready, 1)

            parts = G // KM

            def batch_dots(batch, first=False):
                if not first:
                    pe.wait_ge(dots_spread, batch * G)
                for c in range(NCHUNK):
                    pe.wait_ge(blocks_ready, batch * NCHUNK + c + 1)
                    for k in range(0, KB, KM):
                        i = k // KM % parts
                        at = i * KM * Q
                        last = nc.tensor.matmul(dots[at:at + KM * Q, :, :, :],
                                                weights[:, c * KB + k:c * KB + k + KM, :],
                                                blocks[:, c, :, k * Q:(k + KM) * Q],
                                                start=(c == 0 and k < parts * KM),
                                                stop=(c == NCHUNK - 1 and k >= KB - parts * KM),
                                                tile_position=(0, at))
                    last.then_inc(blocks_used, 1)
                pe.wait_ge(dots_spread, batch * G + G)
                if not first:
                    pe.wait_ge(growth_ready, batch)
                else:
                    pe.wait_ge(masks_built, 4 + P // LP)
                for t in range(TB):
                    for m in range(KM):
                        last = nc.tensor.matmul(turned[:, t, :], spread[:, t, m, :, :], layer_sel[:, m, :],
                                                start=(m == 0), stop=(m == KM - 1))
                last.then_inc(turned_ready, 1)

            batch_dots(0, first=True)
            with pe.Fori(1, n_batches) as n:
                batch_dots(n)


_INS = ["r_inputs", "L0_rec_w", "L0_rec_b"]


def kernel(**inputs):
    import numpy as _np
    import concourse.bacc as _bacc
    from concourse import mybir as _mybir
    from concourse.bass_utils import run_bass_kernel_spmd as _run

    nc = _bacc.Bacc("TRN2", target_bir_lowering=False, num_devices=1)
    arrays, args = {}, []
    for name in _INS:
        a = _np.ascontiguousarray(inputs[name])
        arrays[f"in_{name}_dram"] = a
        args.append(nc.dram_tensor(f"in_{name}_dram", a.shape, _mybir.dt.from_np(a.dtype), kind="ExternalInput").ap())
    shape = tuple(arrays["in_r_inputs_dram"].shape)
    out = nc.dram_tensor("out_0_dram", shape, _mybir.dt.float32, kind="ExternalOutput").ap()
    cross_network(nc, *args, out)
    r = _run(nc, [arrays], core_ids=[0])
    return r.results[0]["out_0_dram"]
```
